# Optimizing a Trainium2 kernel written in Bass

```python
import numpy as np
import jax
import jax.numpy as jnp

def _softmax(x, axis=-1):
    return jax.nn.softmax(x, axis=axis)
def _gelu(x):
    return jax.nn.gelu(x, approximate=True)
def _silu(x):
    return jax.nn.silu(x)
def _sigmoid(x):
    return jax.nn.sigmoid(x)
def _layernorm(x, axis=-1, eps=1e-5):
    m = jnp.mean(x, axis=axis, keepdims=True)
    v = jnp.var(x, axis=axis, keepdims=True)
    return (x - m) / jnp.sqrt(v + eps)
def _scatter_add(tgt, idx, src, axis=0):
    return tgt.at[idx].add(src)
def _segment_sum(src, seg, n):
    return jax.ops.segment_sum(src, seg, n)

kernel_name = 'mk_metaformer_d1_conv_nchw256_59b277'

def setup_inputs(seed: int = 0):
    np.random.seed(seed)
    _w = jnp.asarray
    def _rec_inputs():
        import jax
        import jax.numpy as jnp
        _gk = jax.random.key(seed)
        x = -0.000929 + 1 * jax.random.normal(jax.random.fold_in(_gk, 1), (4, 256, 32, 32), jnp.float32)
        return x
    x = _rec_inputs()
    def _L0_conv_setup():
        import jax, jax.numpy as jnp
        import numpy as np
        RATE_NUM = 8
        MAX_RATE = 256
        C = 256
        key = jax.random.key(seed)
        k1, k2, k3, k4 = jax.random.split(key, 4)
        B, H, W = (4, 32, 32)
        x = jax.random.normal(k1, (B, MAX_RATE, H, W), dtype=jnp.float32)
        indexes = jax.random.randint(k2, (B * H * W,), 0, RATE_NUM, dtype=jnp.int64)
        std = np.sqrt(1.0 / 3.0) / np.sqrt(C)
        weight = jax.random.normal(k3, (RATE_NUM, MAX_RATE, C), dtype=jnp.float32) * std
        bound = 1.0 / np.sqrt(RATE_NUM)
        bias = jax.random.uniform(k4, (RATE_NUM, C), dtype=jnp.float32, minval=-bound, maxval=bound)
        return {'x': x, 'indexes': indexes, 'weight': weight, 'bias': bias}
    _L0_conv_all = _L0_conv_setup()
    _L0_conv_in = {k: v for k, v in _L0_conv_all.items() if k in ('indexes', 'weight', 'bias', )}
    del _L0_conv_all

    def _L0_ffn_setup():
        import jax, jax.numpy as jnp
        import numpy as np
        D_MODEL = 256
        N_EXPERTS = 16
        HIDDEN = 512
        SCALE = 0.02
        key = jax.random.key(seed)
        ks = jax.random.split(key, 5)
        x = jax.random.normal(ks[0], (4, 8192, D_MODEL), dtype=jnp.float32)
        gate_w = jax.random.normal(ks[1], (D_MODEL, N_EXPERTS), dtype=jnp.float32) * SCALE
        gate_b = jnp.zeros((N_EXPERTS,), dtype=jnp.float32)
        w1 = jax.random.normal(ks[2], (N_EXPERTS, D_MODEL, HIDDEN), dtype=jnp.float32) * SCALE
        w2 = jax.random.normal(ks[3], (N_EXPERTS, D_MODEL, HIDDEN), dtype=jnp.float32) * SCALE
        w3 = jax.random.normal(ks[4], (N_EXPERTS, HIDDEN, D_MODEL), dtype=jnp.float32) * SCALE
        return {'x': x, 'gate_w': gate_w, 'gate_b': gate_b, 'w1': w1, 'w2': w2, 'w3': w3}
    _L0_ffn_all = _L0_ffn_setup()
    _L0_ffn_in = {k: v for k, v in _L0_ffn_all.items() if k in ('gate_w', 'gate_b', 'w1', 'w2', 'w3', )}
    del _L0_ffn_all

    return {
        "x": x,
        "L0_conv_indexes": _L0_conv_in["indexes"],
        "L0_conv_weight": _L0_conv_in["weight"],
        "L0_conv_bias": _L0_conv_in["bias"],
        "L0_ffn_gate_w": _L0_ffn_in["gate_w"],
        "L0_ffn_gate_b": _L0_ffn_in["gate_b"],
        "L0_ffn_w1": _L0_ffn_in["w1"],
        "L0_ffn_w2": _L0_ffn_in["w2"],
        "L0_ffn_w3": _L0_ffn_in["w3"],
    }

def reference(x, L0_conv_indexes, L0_conv_weight, L0_conv_bias, L0_ffn_gate_w, L0_ffn_gate_b, L0_ffn_w1, L0_ffn_w2, L0_ffn_w3):
    import jax
    import jax.numpy as jnp
    def _L0_conv_ref(x, indexes, weight, bias):
        import jax, jax.numpy as jnp
        import numpy as np
        RATE_NUM = 8
        MAX_RATE = 256
        C = 256
        B, R, H, W = x.shape
        L = H * W
        x_blr = x.reshape(B, R, L).transpose(0, 2, 1)
        w = weight[indexes].reshape(B, L, R, -1)
        b = bias[indexes].reshape(B, L, -1)
        out = jnp.einsum('blr,blrc->blc', x_blr, w) + b
        return out.reshape(B, H, W, -1).transpose(0, 3, 1, 2)

    def _L0_ffn_ref(x, gate_w, gate_b, w1, w2, w3):
        import jax, jax.numpy as jnp
        import numpy as np
        D_MODEL = 256
        N_EXPERTS = 16
        HIDDEN = 512
        SCALE = 0.02
        n_experts = w1.shape[0]
        logits = jnp.einsum('bsd,de->bse', x, gate_w) + gate_b
        probs = jax.nn.softmax(logits, axis=-1)
        top_probs, top_idx = jax.lax.top_k(probs, 2)
        top_probs = top_probs / jnp.sum(top_probs, axis=-1, keepdims=True)
        dispatch = jnp.sum(jax.nn.one_hot(top_idx, n_experts, dtype=x.dtype) * top_probs[..., None], axis=-2)
        h1 = jnp.einsum('bsd,edh->bseh', x, w1)
        h2 = jnp.einsum('bsd,edh->bseh', x, w2)
        hidden = jax.nn.silu(h1) * h2
        expert_out = jnp.einsum('bseh,eho->bseo', hidden, w3)
        return jnp.einsum('bseo,bse->bso', expert_out, dispatch)

    def _gn(v, G=32, eps=1e-5):
        B_, C_, H_, W_ = v.shape
        g = v.reshape(B_, G, C_ // G, H_, W_)
        m = jnp.mean(g, axis=(2, 3, 4), keepdims=True)
        s = jnp.var(g, axis=(2, 3, 4), keepdims=True)
        return ((g - m) / jnp.sqrt(s + eps)).reshape(v.shape)

    def _ln_c(v, eps=1e-6):
        m = jnp.mean(v, axis=1, keepdims=True)
        s = jnp.var(v, axis=1, keepdims=True)
        return (v - m) / jnp.sqrt(s + eps)

    def _ln_t(v, eps=1e-5):
        m = jnp.mean(v, axis=-1, keepdims=True)
        s = jnp.var(v, axis=-1, keepdims=True)
        return (v - m) / jnp.sqrt(s + eps)

    def _to_tokens(v):
        B_, C_, H_, W_ = v.shape
        return v.reshape(B_, C_, H_ * W_).transpose(0, 2, 1)
    def _from_tokens(t, like):
        B_, C_, H_, W_ = like.shape
        return t.transpose(0, 2, 1).reshape(B_, C_, H_, W_)

    x = x + _L0_conv_ref(_ln_c(x), L0_conv_indexes, L0_conv_weight, L0_conv_bias)
    t = _to_tokens(x)
    t = t + _L0_ffn_ref(_ln_t(t), L0_ffn_gate_w, L0_ffn_gate_b, L0_ffn_w1, L0_ffn_w2, L0_ffn_w3)
    x = _from_tokens(t, x)
    return x


_drawn_inputs = setup_inputs


def setup_inputs(seed=0):
    import zlib

    import numpy as np

    out = dict(_drawn_inputs(seed))
    spreads = {'L0_ffn_gate_b': (0.0, 0.8)}
    factors = {'L0_ffn_gate_w': 4.275, 'L0_ffn_w1': 3.938, 'L0_ffn_w2': 3.893, 'L0_ffn_w3': 3.893}
    for name, (base, spread) in spreads.items():
        noise = np.random.default_rng([zlib.crc32(name.encode()), seed]).standard_normal(out[name].shape)
        drawn = base * np.exp(spread * noise) if base else spread * noise
        out[name] = jnp.asarray(drawn.astype(out[name].dtype))
    for name, factor in factors.items():
        out[name] = (out[name] * factor).astype(out[name].dtype)
    return out
```

```python
from contextlib import ExitStack

import concourse.bass as bass
from concourse import mybir

F32 = mybir.dt.float32
I32 = mybir.dt.int32
U32 = mybir.dt.uint32
ALU = mybir.AluOpType
ACT = mybir.ActivationFunctionType
AX = mybir.AxisListType

P = 128
B, C, L = 4, 256, 1024
TOK = B * L
R = 8
E, HID = 16, 512
CC = C // P
HC = HID // P
TA = TOK // P
SB = (TOK - R) // P + R
SE = (2 * TOK - E) // P + E
CAP = TOK + P
ROW = C + 4
RING = 4
WE = 2 * CC * HID + HC * C
INVALID = 1.0e6
EPS_C, EPS_T = 1e-6, 1e-5


class Step:

    def __init__(self, n, h, p):
        self.n, self.h, self.p = n, h, p


def need(eng, sem, value):
    if isinstance(value, int) and value <= 0:
        return
    eng.wait_ge(sem, value)


def pipeline(eng, steps, unroll, lead, lag, body):

    def iteration(base, u):
        def at(k):
            d, p = divmod(u - k, unroll)
            if isinstance(base, int):
                n = base * unroll + u - k
                return Step(n, base + d, p) if 0 <= n < steps else None
            return Step(base * unroll + (u - k), base + d, p)
        body(at)

    first = -(-lag // unroll) + 1
    last = (steps - lead) // unroll
    for i in range(-lead, first * unroll):
        iteration(i // unroll, i % unroll)
    if last > first:
        with eng.Fori(first, last) as h:
            for u in range(unroll):
                iteration(h, u)
    for i in range(max(last, first) * unroll, steps + lag):
        iteration(i // unroll, i % unroll)


def metaformer_layer(nc, x, indexes, conv_w, conv_b, gate_w, gate_b, w1, w2, w3, out):
    with ExitStack() as ctx:
        def sb(name, shape, dt=F32):
            return ctx.enter_context(nc.sbuf_tensor(name, shape, dt))

        def psum(name, shape):
            return ctx.enter_context(nc.psum_tensor(name, shape, F32))

        def sem(name):
            return ctx.enter_context(nc.semaphore(name))

        def scratch(name, rows, cols):
            return nc.dram_tensor(name, (rows, cols), F32, kind="Internal").ap()

        conv_rows = scratch("conv_rows", (SB + R) * P, ROW)
        t_rows = scratch("t_rows", SB * P, C)
        ffn_rows = scratch("ffn_rows", (E + 1) * CAP, ROW)
        y_rows = scratch("y_rows", 2 * TOK, C)

        ident = sb("ident", [P, P])
        before = sb("before", [P, P])
        ones = sb("ones", [P, P])
        iota_r = sb("iota_r", [P, R])
        iota_e = sb("iota_e", [P, E])
        iota_s = sb("iota_s", [P, SE])
        expert_base = sb("expert_base", [P, E])
        pad_base = sb("pad_base", [P, E + 1])
        tok_id = sb("tok_id", [P, TA])
        zero_rows = sb("zero_rows", [P, ROW])
        pad_row = sb("pad_row", [P, ROW])
        eps_c = sb("eps_c", [P, 1])
        eps_t = sb("eps_t", [P, 1])
        cw = sb("cw", [P, CC, R, C])
        cb = sb("cb", [1, R, C])
        gw = sb("gw", [P, CC, E])
        gb = sb("gb", [P, E])
        ring = sb("ring", [P, RING, WE])
        idx_i = sb("idx_i", [TA, P], I32)
        idx_f = sb("idx_f", [TA, P])
        idx_t = sb("idx_t", [P, TA, 1])
        c_one = sb("c_one", [P, TA, R])
        c_tot = sb("c_tot", [P, R, TA])
        c_inc = sb("c_inc", [P, R, TA])
        c_ones = sb("c_ones", [P, R * TA])
        c_q = sb("c_q", [P, TA, R])
        c_q2 = sb("c_q2", [P, TA, R])
        c_pos = sb("c_pos", [P, TA])
        c_pos_i = sb("c_pos_i", [P, TA], I32)
        c_n = sb("c_n", [P, R])
        c_st = sb("c_st", [P, R])
        c_ti = sb("c_ti", [P, R], I32)
        c_ti2 = sb("c_ti2", [P, R], I32)
        c_tf = sb("c_tf", [P, R])
        c_ci = sb("c_ci", [P, R])
        c_bs = sb("c_bs", [P, R])
        c_sh = sb("c_sh", [P, R])
        c_far = sb("c_far", [P, R])
        c_none = sb("c_none", [P, R])
        c_last = sb("c_last", [P, R])
        c_last_i = sb("c_last_i", [P, R], I32)
        c_cmp = sb("c_cmp", [P, SB, R])
        c_sel = sb("c_sel", [P, SB])
        c_sel_i = sb("c_sel_i", [P, SB], I32)
        x_in = sb("x_in", [P, 4, CC, P])
        a_row = sb("a_row", [P, 4, ROW])
        a_pi = sb("a_pi", [P, 4, 1], I32)
        a_st = sb("a_st", [P, 4, 6])
        a_mv = sb("a_mv", [P, 4, 2])
        a_sd = sb("a_sd", [P, 4, 1])
        b_row = sb("b_row", [P, 4, ROW])
        b_xh = sb("b_xh", [P, 4, C])
        b_xT = sb("b_xT", [P, 4, C])
        b_t = sb("b_t", [P, 4, C])
        b_st = sb("b_st", [P, 4, 6])
        b_mv = sb("b_mv", [P, 4, 2])
        b_sd = sb("b_sd", [P, 4, 1])
        b_rs = sb("b_rs", [P, 4, 1])
        b_nm = sb("b_nm", [P, 4, 1])
        b_th = sb("b_th", [P, 4, ROW])
        b_tT = sb("b_tT", [P, 4, C])
        b_lg = sb("b_lg", [P, 4, E])
        b_m8 = sb("b_m8", [P, 4, 8])
        b_i8 = sb("b_i8", [P, 4, 8], U32)
        b_bad = sb("b_bad", [P, 4, 1])
        b_if = sb("b_if", [P, 4, 2])
        b_one = sb("b_one", [P, 4, 2, E])
        b_cnt = sb("b_cnt", [P, 4, E])
        b_acc = sb("b_acc", [P, 4, E])
        b_pr = sb("b_pr", [P, 4, E])
        b_pq = sb("b_pq", [P, 4, 2, E])
        b_ps = sb("b_ps", [P, 4, 2])
        b_pi = sb("b_pi", [P, 4, 2], I32)
        e_n = sb("e_n", [P, E + 1])
        e_pad = sb("e_pad", [P, E + 1], I32)
        e_ti = sb("e_ti", [P, E], I32)
        e_t2 = sb("e_t2", [P, E], I32)
        e_tf = sb("e_tf", [P, E])
        e_inc = sb("e_inc", [P, E])
        e_inc_i = sb("e_inc_i", [P, E], I32)
        e_cmp = sb("e_cmp", [P, SE, E])
        e_cmt = sb("e_cmt", [P, SE, E])
        e_of = sb("e_of", [P, SE])
        e_clip = sb("e_clip", [P, SE])
        e_st = sb("e_st", [P, SE])
        e_j = sb("e_j", [P, SE])
        e_real = sb("e_real", [P, SE])
        e_j2 = sb("e_j2", [P, SE])
        e_adr = sb("e_adr", [P, SE])
        e_ad2 = sb("e_ad2", [P, SE])
        e_clip_i = sb("e_clip_i", [P, SE], I32)
        e_slot_i = sb("e_slot_i", [P, SE], I32)
        e_adr_i = sb("e_adr_i", [P, SE], I32)
        f_row = sb("f_row", [P, 4, ROW])
        f_k1 = sb("f_k1", [P, 4, 1])
        f_sg = sb("f_sg", [P, 4, 1])
        f_ds = sb("f_ds", [P, 4, 1])
        f_di = sb("f_di", [P, 4, 1], I32)
        f_th = sb("f_th", [P, 4, 1])
        f_g = sb("f_g", [P, 4, 1])
        f_xT = sb("f_xT", [P, 2, C])
        f_sil = sb("f_sil", [P, 2, HID])
        f_hid = sb("f_hid", [P, 2, HID])
        f_hT = sb("f_hT", [P, 2, HID])
        f_y = sb("f_y", [P, 4, C])
        t_tok = sb("t_tok", [P, TA, C])
        o_y1 = sb("o_y1", [P, 4, C])
        o_y2 = sb("o_y2", [P, 4, C])
        o_s = sb("o_s", [P, 4, C])
        o_r = sb("o_r", [P, 4, C])
        o_T = cw[:, 0].rearrange("p r n -> p (r n)").rearrange("p (b c t l) -> p b c t l", b=2, c=CC, t=4)

        ps_x = [psum(f"ps_x{i}", [P, 512]) for i in range(2)]
        ps_c = [psum(f"ps_c{i}", [P, 512]) for i in range(2)]
        ps_t = [psum(f"ps_t{i}", [P, 512]) for i in range(2)]
        ps_g = psum("ps_g", [P, 512])
        ps_r = psum("ps_r", [P, 512])
        ps_h1, ps_h2, ps_hT = ps_t[0], ps_t[1], ps_g

        zeroed = sem("zeroed")
        consts = sem("consts")
        idx_in = sem("idx_in")
        cw_in, gw_in = sem("cw_in"), sem("gw_in")
        tail_zero = sem("tail_zero")
        rt = sem("rt")
        idx_tr, rank_c = sem("idx_tr"), sem("rank_c")
        conv_table = sem("conv_table")
        x_ready = [sem(f"x_ready{i}") for i in range(4)]
        a_tr, a_copied, a_stat, a_mean = sem("a_tr"), sem("a_copied"), sem("a_stat"), sem("a_mean")
        a_std, a_rstd, a_meta = sem("a_std"), sem("a_rstd"), sem("a_meta")
        a_sent = [sem(f"a_sent{i}") for i in range(4)]
        b_in = [sem(f"b_in{i}") for i in range(4)]
        b_norm, b_xtr, b_xcp, b_conv = sem("b_norm"), sem("b_xtr"), sem("b_xcp"), sem("b_conv")
        b_tsum, b_stat, b_mean, b_std = sem("b_tsum"), sem("b_stat"), sem("b_mean"), sem("b_std")
        b_rstd, b_nmr, b_thd, b_ttr, b_tcp = (sem("b_rstd"), sem("b_nmr"), sem("b_thd"),
                                              sem("b_ttr"), sem("b_tcp"))
        b_gate, b_log, b_max, b_idx = sem("b_gate"), sem("b_log"), sem("b_max"), sem("b_idx")
        b_wrong, b_idf, b_hot, b_cn, b_ac = (sem("b_wrong"), sem("b_idf"), sem("b_hot"),
                                             sem("b_cn"), sem("b_ac"))
        b_rank, b_prs, b_pqs, b_pos, b_posi = (sem("b_rank"), sem("b_prs"), sem("b_pqs"),
                                               sem("b_pos"), sem("b_posi"))
        b_meta = sem("b_meta")
        b_sent = [sem(f"b_sent{i}") for i in range(4)]
        t_out = [sem(f"t_out{i}") for i in range(4)]
        totals, et = sem("totals"), sem("et")
        pads_known, table_known = sem("pads_known"), sem("table_known")
        pads_sent = sem("pads_sent")
        w_in = [sem(f"w_in{i}") for i in range(RING)]
        w_ready = sem("w_ready")
        f_in = [sem(f"f_in{i}") for i in range(4)]
        f_kd, f_sgd, f_dsd, f_did = sem("f_kd"), sem("f_sgd"), sem("f_dsd"), sem("f_did")
        f_thd, f_gd = sem("f_thd"), sem("f_gd")
        f_xtr, f_xcp, f_h1d, f_h2d = sem("f_xtr"), sem("f_xcp"), sem("f_h1d"), sem("f_h2d")
        f_sild, f_hidd, f_htr, f_hcp = sem("f_sild"), sem("f_hidd"), sem("f_htr"), sem("f_hcp")
        f_ymm, f_yd = sem("f_ymm"), sem("f_yd")
        f_sent = [sem(f"f_sent{i}") for i in range(4)]
        t_back = sem("t_back")
        o_in = [sem(f"o_in{i}") for i in range(4)]
        o_sd, o_rd, o_tr, o_cp = sem("o_sd"), sem("o_rd"), sem("o_tr"), sem("o_cp")
        o_out = [sem(f"o_out{i}") for i in range(2)]

        def value(eng, n):
            return n if isinstance(n, int) else nc.snap(n, engines=[eng.engine])

        def own_wait(eng):
            eng.wait_ge(consts, 1)

        x_v = x.rearrange("b (c p) h w -> b p c (h w)", p=P)
        out_v = out.rearrange("b (c p) h w -> b p c (h w)", p=P)
        w1_ring = ring[:, :, 0:CC * HID].rearrange("p s (c n) -> p s c n", c=CC)
        w2_ring = ring[:, :, CC * HID:2 * CC * HID].rearrange("p s (c n) -> p s c n", c=CC)
        w3_ring = ring[:, :, 2 * CC * HID:WE].rearrange("p s (c n) -> p s c n", c=HC)
        w1_v = w1.rearrange("e (c p) n -> e p c n", p=P)
        w2_v = w2.rearrange("e (c p) n -> e p c n", p=P)
        w3_v = w3.rearrange("e (c p) n -> e p c n", p=P)

        block = ctx.enter_context(nc.Block())

        @block.sync
        def _(sp):
            sp.dma_start(idx_i[:], indexes.rearrange("(t p) -> t p", p=P)).then_inc(idx_in, 16)

            def load_x(b, t, n, h):
                if not isinstance(n, int) or n >= 4:
                    need(sp, a_tr, n - 3)
                sp.dma_start(x_in[:, t % 4], x_v[b, :, :, t * P:(t + 1) * P]).then_inc(x_ready[t % 4], 16)

            for t in range(4):
                load_x(0, t, t, 0)
            for c in range(CC):
                sp.dma_start(cw[:, c], conv_w[:, c * P:(c + 1) * P, :].rearrange("r p n -> p r n")).then_inc(cw_in, 16)
            sp.dma_start(cb[:], conv_b.rearrange("(a r) n -> a r n", a=1)).then_inc(cw_in, 16)
            sp.dma_start(gw[:], gate_w.rearrange("(c p) e -> p c e", p=P)).then_inc(gw_in, 16)
            sp.dma_start(gb[:], gate_b.rearrange("(a e) -> a e", a=1).to_broadcast([P, E])).then_inc(gw_in, 16)
            sp.wait_ge(consts, 1)
            for s in range(TA, SB):
                sp.dma_start(conv_rows[s * P:(s + 1) * P, :], zero_rows[:]).then_inc(tail_zero, 16)
            sp.wait_ge(conv_table, 1)
            sp.wait_ge(tail_zero, 16 * (SB - TA))
            for r in range(R):
                tile = sp.value_load(c_last_i[0:1, r:r + 1], min_val=0, max_val=SB + R - 1)
                sp.dma_start(conv_rows[bass.ds(tile * P, P), :], zero_rows[:]).then_inc(tail_zero, 16)
            for t in range(4, 8):
                load_x(0, t, t, 0)
            with sp.Fori(1, B) as b:
                for t in range(8):
                    load_x(b, t, b * 8 + t, b * 2 + t // 4)

            def load_expert(e, slot):
                sp.dma_start(w1_ring[:, slot], w1_v[e]).then_inc(w_in[slot], 16)
                sp.dma_start(w2_ring[:, slot], w2_v[e]).then_inc(w_in[slot], 16)
                sp.dma_start(w3_ring[:, slot], w3_v[e]).then_inc(w_in[slot], 16)

            for e in range(RING):
                load_expert(e, e)

            for i in range(4):
                sp.wait_ge(a_sent[i], 16 * (TA // 4))
            def conv_rows_in(at):
                j = at(-3)
                if j:
                    need(sp, b_tsum, j.n - 3)
                    need(sp, b_meta, j.n - 3)
                    sp.dma_start(b_row[:, j.p], conv_rows[bass.ds(j.n * P, P), :]).then_inc(b_in[j.p], 16)
                j = at(0)
                if j:
                    need(sp, b_tsum, j.n + 1)
                    sp.dma_start(t_rows[bass.ds(j.n * P, P), :], b_t[:, j.p]).then_inc(t_out[j.p], 16)

            pipeline(sp, SB, 4, 3, 0, conv_rows_in)

            for e in range(RING):
                sp.wait_ge(w_in[e], 48)
                sp.sem_inc(w_ready, 1)
            sp.wait_ge(table_known, 1)
            with sp.Fori(1, E // RING) as q:
                for u in range(RING):
                    last = sp.value_load(e_inc_i[0:1, bass.ds(q * RING + (u - RING), 1)], min_val=1, max_val=SE)
                    sp.wait_ge(f_ymm, last)
                    load_expert(bass.ds(q * RING + u, 1), u)
                    sp.wait_ge(w_in[u], q * 48 + 48)
                    sp.sem_inc(w_ready, 1)

            for i in range(4):
                sp.wait_ge(f_sent[i], 16 * ((SE + 3 - i) // 4))

            def y_in(at):
                j = at(-3)
                if j:
                    need(sp, o_rd, j.n - 3)
                    sp.dma_start(o_y1[:, j.p], y_rows[bass.ds(j.n * P, P), :]).then_inc(o_in[j.p], 16)
                    sp.dma_start(o_y2[:, j.p], y_rows[bass.ds(j.n * P + TOK, P), :]).then_inc(o_in[j.p], 16)

            pipeline(sp, TA, 4, 3, 0, y_in)

        @block.gpsimd
        def _(pool):
            pool.memset(zero_rows[:], 0.0).then_inc(consts, 1)
            pool.memset(ident[:], 0.0).then_inc(zeroed, 1)
            pool.memset(ones[:], 1.0).then_inc(zeroed, 1)
            pool.memset(pad_row[:, 0:C], 0.0).then_inc(consts, 1)
            pool.memset(pad_row[:, C:C + 1], 2.0 * TOK).then_inc(consts, 1)
            pool.memset(pad_row[:, C + 1:ROW], 0.0).then_inc(consts, 1)
            pool.memset(a_row[:, :, C + 1:C + 2], 1.0).then_inc(consts, 1)
            pool.memset(c_ones[:], 1.0).then_inc(consts, 1)
            pool.memset(eps_c[:], EPS_C).then_inc(consts, 1)
            pool.memset(eps_t[:], EPS_T).then_inc(consts, 1)
            pool.memset(b_th[:, :, C + 3:ROW], 0.0).then_inc(consts, 1)
            pool.memset(b_acc[:], 0.0).then_inc(consts, 1)
            pool.memset(e_n[:], 0.0).then_inc(consts, 1)
            flt = dict(allow_small_or_imprecise_dtypes=True)
            pool.iota(iota_r[:], pattern=[[1, R]], base=0, channel_multiplier=0, **flt).then_inc(consts, 1)
            pool.iota(iota_e[:], pattern=[[1, E]], base=0, channel_multiplier=0, **flt).then_inc(consts, 1)
            pool.iota(iota_s[:], pattern=[[1, SE]], base=0, channel_multiplier=0, **flt).then_inc(consts, 1)
            pool.iota(expert_base[:], pattern=[[CAP, E]], base=0, channel_multiplier=0, **flt).then_inc(consts, 1)
            pool.iota(pad_base[:], pattern=[[CAP, E + 1]], base=0, channel_multiplier=1, **flt).then_inc(consts, 1)
            pool.iota(tok_id[:], pattern=[[P, TA]], base=0, channel_multiplier=1, **flt).then_inc(consts, 1)
            pool.wait_ge(zeroed, 2)
            pool.affine_select(out=ident[:], in_=ident[:], compare_op=ALU.not_equal, fill=1.0, base=0,
                               pattern=[[-1, P]], channel_multiplier=1).then_inc(consts, 1)
            pool.affine_select(out=before[:], in_=ones[:], compare_op=ALU.is_gt, fill=0.0, base=0,
                               pattern=[[1, P]], channel_multiplier=-1).then_inc(consts, 1)

            pool.wait_ge(tail_zero, 16 * (SB - TA + R))

            def scatter_conv(at):
                j = at(1)
                if j:
                    done = value(pool, j.n + 1)
                    own_wait(pool)
                    pool.wait_ge(a_copied, done)
                    pool.wait_ge(a_meta, done)
                    pool.indirect_dma_start(
                        out=conv_rows,
                        out_offset=bass.IndirectOffsetOnAxis(ap=a_pi[:, j.p], axis=0),
                        in_=a_row[:, j.p], in_offset=None).then_inc(a_sent[j.p], 16)

            pipeline(pool, TA, 4, 0, 1, scatter_conv)

            def scatter_ffn(at):
                j = at(2)
                if j:
                    done = value(pool, j.n + 1)
                    own_wait(pool)
                    pool.wait_ge(b_thd, done)
                    pool.wait_ge(b_meta, done)
                    pool.wait_ge(b_posi, done)
                    for k in range(2):
                        pool.indirect_dma_start(
                            out=ffn_rows,
                            out_offset=bass.IndirectOffsetOnAxis(ap=b_pi[:, j.p, k:k + 1], axis=0),
                            in_=b_th[:, j.p], in_offset=None, bounds_check=(E + 1) * CAP - 1,
                            oob_is_err=False).then_inc(b_sent[j.p], 16)

            pipeline(pool, SB, 4, 0, 2, scatter_ffn)
            pool.wait_ge(pads_known, 1)
            for e in range(E + 1):
                pool.indirect_dma_start(
                    out=ffn_rows, out_offset=bass.IndirectOffsetOnAxis(ap=e_pad[:, e:e + 1], axis=0),
                    in_=pad_row[:], in_offset=None).then_inc(pads_sent, 16)
            for i in range(4):
                pool.wait_ge(t_out[i], 16 * ((SB + 3 - i) // 4))

            def scatter_y(at):
                j = at(1)
                if j:
                    done = value(pool, j.n + 1)
                    own_wait(pool)
                    pool.wait_ge(f_did, done)
                    pool.wait_ge(f_yd, done)
                    pool.indirect_dma_start(
                        out=y_rows, out_offset=bass.IndirectOffsetOnAxis(ap=f_di[:, j.p], axis=0),
                        in_=f_y[:, j.p], in_offset=None, bounds_check=2 * TOK - 1,
                        oob_is_err=False).then_inc(f_sent[j.p], 16)

            for t in range(TA):
                pool.indirect_dma_start(
                    out=t_tok[:, t], out_offset=None, in_=t_rows,
                    in_offset=bass.IndirectOffsetOnAxis(ap=c_pos_i[:, t:t + 1], axis=0)).then_inc(t_back, 16)
            pipeline(pool, SE, 4, 0, 1, scatter_y)

        @block.tensor
        def _(pe):
            pe.wait_ge(consts, 19)
            pe.wait_ge(rt, 1)
            pe.transpose(ps_x[0][:, 0:TA], idx_f[:], ident[0:TA, 0:TA]).then_inc(idx_tr, 1)
            pe.wait_ge(rt, 3)
            hot = c_one[:].rearrange("p t r -> p (t r)")
            pe.matmul(ps_c[0][:, 0:TA * R], before[:], hot, start=True, stop=True)
            pe.matmul(ps_t[0][:, 0:TA * R], ones[:], hot, start=True, stop=True).then_inc(rank_c, 1)

            def transpose_x(at):
                j = at(0)
                if j:
                    pe.wait_ge(x_ready[j.p], j.h * 16 + 16)
                    need(pe, a_copied, j.n - 1)
                    for c in range(CC):
                        last = pe.transpose(ps_x[j.p % 2][:, c * P:(c + 1) * P],
                                            x_in[:, j.p, c], ident[:])
                    last.then_inc(a_tr, 1)

            pipeline(pe, TA, 4, 0, 0, transpose_x)
            pe.wait_ge(cw_in, 16 * (CC + 1))
            pe.wait_ge(gw_in, 32)
            pe.wait_ge(a_copied, TA)

            def conv_and_gate(at):
                j = at(-1)
                if j:
                    pe.wait_ge(b_norm, j.n + 1)
                    need(pe, b_xcp, j.n - 1)
                    for c in range(CC):
                        last = pe.transpose(ps_x[j.p % 2][:, c * P:(c + 1) * P],
                                            b_xh[:, j.p, c * P:(c + 1) * P], ident[:])
                    last.then_inc(b_xtr, 1)
                j = at(1)
                if j:
                    pe.wait_ge(b_thd, j.n + 1)
                    need(pe, b_tcp, j.n - 1)
                    for c in range(CC):
                        last = pe.transpose(ps_t[j.p % 2][:, c * P:(c + 1) * P],
                                            b_th[:, j.p, c * P:(c + 1) * P], ident[:])
                    last.then_inc(b_ttr, 1)
                j = at(0)
                if j:
                    r = pe.value_load(c_sel_i[0:1, bass.ds(j.n, 1)], min_val=0, max_val=R - 1)
                    acc = ps_c[j.p % 2][:, 0:C]
                    need(pe, b_tsum, j.n - 1)
                    pe.matmul(acc, ones[0:1, :], cb[:, bass.ds(r, 1), :].rearrange("p a n -> p (a n)"),
                              start=True, stop=False)
                    pe.wait_ge(b_xcp, j.n + 1)
                    for c in range(CC):
                        last = pe.matmul(acc, b_xT[:, j.p, c * P:(c + 1) * P],
                                         cw[:, c, bass.ds(r, 1), :].rearrange("p a n -> p (a n)"),
                                         start=False, stop=(c == CC - 1))
                    last.then_inc(b_conv, 1)
                j = at(1)
                if j:
                    pe.wait_ge(b_tcp, j.n + 1)
                    need(pe, b_log, j.n)
                    for c in range(CC):
                        last = pe.matmul(ps_g[:, 0:E], b_tT[:, j.p, c * P:(c + 1) * P],
                                         gw[:, c], start=(c == 0), stop=(c == CC - 1))
                    last.then_inc(b_gate, 1)
                j = at(2)
                if j:
                    pe.wait_ge(b_cn, j.n + 1)
                    need(pe, b_ac, j.n)
                    need(pe, b_prs, j.n)
                    rank = ps_r[:, 0:E]
                    pe.matmul(rank, before[:], b_cnt[:, j.p], start=True, stop=False)
                    pe.matmul(rank, ones[:], b_acc[:, (j.p + 3) % 4], start=False,
                              stop=True).then_inc(b_rank, 1)

            pipeline(pe, SB, 4, 1, 2, conv_and_gate)
            pe.wait_ge(b_ac, SB)
            pe.wait_ge(b_prs, SB)
            pe.matmul(ps_r[:, 0:E], ones[:], b_acc[:, (SB - 1) % 4], start=True,
                      stop=True).then_inc(totals, 1)
            pe.wait_ge(table_known, 1)
            pe.wait_ge(b_tsum, SB)

            def expert(at):
                j = at(-1)
                if j:
                    pe.wait_ge(f_in[j.p], j.h * 16 + 16)
                    need(pe, f_xcp, j.n - 1)
                    for c in range(CC):
                        last = pe.transpose(ps_x[j.p % 2][:, c * P:(c + 1) * P],
                                            f_row[:, j.p, c * P:(c + 1) * P], ident[:])
                    last.then_inc(f_xtr, 1)
                j = at(0)
                if j:
                    e = pe.value_load(e_clip_i[0:1, bass.ds(j.n, 1)], min_val=0, max_val=E - 1)
                    slot = pe.value_load(e_slot_i[0:1, bass.ds(j.n, 1)], min_val=0, max_val=RING - 1)
                    pe.wait_ge(w_ready, e + 1)
                    pe.wait_ge(f_xcp, j.n + 1)
                    need(pe, f_sild, j.n)
                    for c in range(CC):
                        last = pe.matmul(ps_h1[:], f_xT[:, j.p % 2, c * P:(c + 1) * P],
                                         w1_ring[:, bass.ds(slot, 1), c].rearrange("p a n -> p (a n)"),
                                         start=(c == 0), stop=(c == CC - 1))
                    last.then_inc(f_h1d, 1)
                i = at(1)
                if i:
                    pe.wait_ge(f_hidd, i.n + 1)
                    need(pe, f_hcp, i.n)
                    for c in range(HC):
                        last = pe.transpose(ps_hT[:, c * P:(c + 1) * P], f_hid[:, i.p % 2, c * P:(c + 1) * P], ident[:])
                    last.then_inc(f_htr, 1)
                if j:
                    need(pe, f_hidd, j.n)
                    for c in range(CC):
                        last = pe.matmul(ps_h2[:], f_xT[:, j.p % 2, c * P:(c + 1) * P],
                                         w2_ring[:, bass.ds(slot, 1), c].rearrange("p a n -> p (a n)"),
                                         start=(c == 0), stop=(c == CC - 1))
                    last.then_inc(f_h2d, 1)
                if i:
                    slot_i = pe.value_load(e_slot_i[0:1, bass.ds(i.n, 1)], min_val=0, max_val=RING - 1)
                    pe.wait_ge(f_hcp, i.n + 1)
                    need(pe, f_yd, i.n - 1)
                    for c in range(HC):
                        last = pe.matmul(ps_c[i.p % 2][:, 0:C], f_hT[:, i.p % 2, c * P:(c + 1) * P],
                                         w3_ring[:, bass.ds(slot_i, 1), c].rearrange("p a n -> p (a n)"),
                                         start=(c == 0), stop=(c == HC - 1))
                    last.then_inc(f_ymm, 1)

            pipeline(pe, SE, 4, 1, 1, expert)

            def transpose_out(at):
                j = at(0)
                if j:
                    pe.wait_ge(o_rd, j.n + 1)
                    need(pe, o_cp, j.n - 1)
                    for c in range(CC):
                        last = pe.transpose(ps_t[j.p % 2][:, c * P:(c + 1) * P],
                                            o_r[:, j.p, c * P:(c + 1) * P], ident[:])
                    last.then_inc(o_tr, 1)

            pipeline(pe, TA, 4, 0, 0, transpose_out)

        @block.scalar
        def _(act):
            act.wait_ge(consts, 19)

            def rows_a(at):
                j = at(0)
                if j:
                    act.wait_ge(a_tr, j.n + 1)
                    if not (isinstance(j.n, int) and j.n < 4):
                        act.wait_ge(a_sent[j.p], j.h * 16)
                    nc.scalar.copy(a_row[:, j.p, 0:C], ps_x[j.p % 2][:, 0:C]).then_inc(a_copied, 1)
                j = at(1)
                if j:
                    act.wait_ge(a_mean, j.n + 1)
                    need(act, a_rstd, j.n - 3)
                    nc.scalar.activation(a_sd[:, j.p], a_mv[:, j.p, 1:2], ACT.Sqrt, bias=eps_c[:]).then_inc(a_std, 1)

            pipeline(act, TA, 4, 0, 1, rows_a)

            def rows_b(at):
                j = at(-1)
                if j:
                    act.wait_ge(b_in[j.p], j.h * 16 + 16)
                    need(act, b_xtr, j.n - 3)
                    nc.scalar.activation(b_xh[:, j.p], b_row[:, j.p, 0:C], ACT.Identity,
                                         scale=b_row[:, j.p, C + 2:C + 3],
                                         bias=b_row[:, j.p, C + 3:C + 4]).then_inc(b_norm, 1)
                    act.wait_ge(b_xtr, j.n + 1)
                    need(act, b_conv, j.n - 3)
                    nc.scalar.copy(b_xT[:, j.p], ps_x[j.p % 2][:, 0:C]).then_inc(b_xcp, 1)
                j = at(0)
                if j:
                    act.wait_ge(b_mean, j.n + 1)
                    need(act, b_rstd, j.n - 3)
                    nc.scalar.activation(b_sd[:, j.p], b_mv[:, j.p, 1:2], ACT.Sqrt, bias=eps_t[:]).then_inc(b_std, 1)
                    act.wait_ge(b_nmr, j.n + 1)
                    if not (isinstance(j.n, int) and j.n < 4):
                        act.wait_ge(b_sent[j.p], j.h * 32)
                    nc.scalar.activation(b_th[:, j.p, 0:C], b_t[:, j.p], ACT.Identity, scale=b_rs[:, j.p],
                                         bias=b_nm[:, j.p]).then_inc(b_thd, 1)

            pipeline(act, SB, 4, 1, 0, rows_b)
            act.wait_ge(table_known, 1)
            act.wait_ge(pads_sent, 16 * (E + 1))
            for i in range(4):
                act.wait_ge(b_sent[i], 32 * ((SB + 3 - i) // 4))

            def expert_act(at):
                j = at(-2)
                if j:
                    adr = act.value_load(e_adr_i[0:1, bass.ds(j.n, 1)], min_val=0, max_val=E * CAP)
                    need(act, f_xtr, j.n - 3)
                    need(act, f_did, j.n - 3)
                    need(act, f_thd, j.n - 3)
                    act.dma_start(f_row[:, j.p], ffn_rows[bass.ds(adr, P), :]).then_inc(f_in[j.p], 16)
                j = at(0)
                if j:
                    act.wait_ge(f_h1d, j.n + 1)
                    need(act, f_hidd, j.n - 1)
                    nc.scalar.activation(f_sil[:, j.p % 2], ps_h1[:], ACT.Silu).then_inc(f_sild, 1)
                    act.wait_ge(f_sgd, j.n + 1)
                    need(act, f_gd, j.n - 3)
                    nc.scalar.activation(f_th[:, j.p], f_row[:, j.p, C + 2:C + 3], ACT.Tanh,
                                         scale=f_sg[:, j.p]).then_inc(f_thd, 1)
                j = at(1)
                if j:
                    act.wait_ge(f_htr, j.n + 1)
                    need(act, f_ymm, j.n - 1)
                    nc.scalar.copy(f_hT[:, j.p % 2], ps_hT[:]).then_inc(f_hcp, 1)

            pipeline(act, SE, 4, 2, 1, expert_act)

            def out_tile(j, buf, group_before):
                act.wait_ge(o_tr, j.n + 1)
                if j.p == 0 and group_before is not None:
                    act.wait_ge(o_out[buf], group_before)
                nc.scalar.copy(o_T[:, buf, :, j.p],
                               ps_t[j.p % 2][:, 0:C].rearrange("p (c l) -> p c l", c=CC)
                               ).then_inc(o_cp, 1)

            def image(b):
                for buf in range(2):
                    for p in range(4):
                        h = b * 2 + buf
                        before_it = None if isinstance(b, int) and b == 0 else b * 16
                        out_tile(Step(h * 4 + p, h, p), buf, before_it)
                    act.wait_ge(o_cp, b * 8 + (4 * buf + 4))
                    act.dma_start(out_v[b, :, :, buf * 512:(buf + 1) * 512],
                                  o_T[:, buf].rearrange("p c t l -> p c (t l)")).then_inc(o_out[buf], 16)

            image(0)
            with act.Fori(1, B) as b:
                image(b)
            for buf in range(2):
                act.wait_ge(o_out[buf], 16 * B)

        @block.vector
        def _(dve):
            v = nc.vector
            dve.wait_ge(idx_in, 16)
            v.tensor_copy(idx_f[:], idx_i[:]).then_inc(rt, 1)
            dve.wait_ge(idx_tr, 1)
            v.tensor_copy(idx_t[:, :, 0], ps_x[0][:, 0:TA]).then_inc(rt, 1)
            dve.wait_ge(rt, 2)
            dve.wait_ge(consts, 19)
            v.tensor_tensor(c_one[:], idx_t[:].to_broadcast([P, TA, R]),
                            iota_r[:].rearrange("p (a r) -> p a r", a=1).to_broadcast([P, TA, R]),
                            ALU.is_equal).then_inc(rt, 1)
            dve.wait_ge(rank_c, 1)
            v.tensor_copy(c_tot[:], ps_t[0][:, 0:TA * R].rearrange("p (t r) -> p r t", r=R)).then_inc(rt, 1)
            dve.wait_ge(rt, 4)
            v.tensor_tensor_scan(c_inc[:].rearrange("p r t -> p (r t)"), c_ones[:],
                                 c_tot[:].rearrange("p r t -> p (r t)"), 0.0, ALU.mult, ALU.add).then_inc(rt, 1)
            dve.wait_ge(rt, 5)
            v.memset(c_st[:, 0:1], 0.0).then_inc(rt, 1)
            v.tensor_copy(c_st[:, 1:R], c_inc[:, 0:R - 1, TA - 1]).then_inc(rt, 1)
            dve.wait_ge(rt, 7)
            v.tensor_tensor(c_n[:], c_inc[:, :, TA - 1], c_st[:], ALU.subtract).then_inc(rt, 1)
            dve.wait_ge(rt, 8)
            v.tensor_scalar(c_ti[:], c_n[:], float(P - 1), None, ALU.add).then_inc(rt, 1)
            dve.wait_ge(rt, 9)
            v.tensor_scalar(c_ti2[:], c_ti[:], 7, None, ALU.arith_shift_right).then_inc(rt, 1)
            dve.wait_ge(rt, 10)
            v.tensor_copy(c_tf[:], c_ti2[:]).then_inc(rt, 1)
            dve.wait_ge(rt, 11)
            v.tensor_tensor_scan(c_ci[:], c_ones[:, 0:R], c_tf[:], 0.0, ALU.mult, ALU.add).then_inc(rt, 1)
            dve.wait_ge(rt, 12)
            v.tensor_tensor(c_bs[:], c_ci[:], c_tf[:], ALU.subtract).then_inc(rt, 1)
            v.scalar_tensor_tensor(out=c_far[:], in0=iota_r[:], scalar=float(SB + 1), in1=c_ci[:], op0=ALU.add,
                                   op1=ALU.subtract).then_inc(rt, 1)
            v.tensor_scalar(c_none[:], c_tf[:], 1.0, None, ALU.is_lt)
            v.tensor_tensor(c_cmp[:], c_ci[:].rearrange("p (a r) -> p a r", a=1).to_broadcast([P, SB, R]),
                            iota_s[:, 0:SB].rearrange("p (s a) -> p s a", a=1).to_broadcast([P, SB, R]),
                            ALU.is_le).then_inc(rt, 1)
            dve.wait_ge(rt, 15)
            v.tensor_tensor(c_last[:], c_far[:], c_none[:], ALU.mult).then_inc(rt, 1)
            v.scalar_tensor_tensor(out=c_sh[:], in0=c_bs[:], scalar=float(P), in1=c_st[:], op0=ALU.mult,
                                   op1=ALU.subtract).then_inc(rt, 1)
            v.tensor_reduce(c_sel[:], c_cmp[:], AX.X, ALU.add).then_inc(rt, 1)
            v.tensor_tensor(c_q[:], c_inc[:].rearrange("p r t -> p t r"), c_tot[:].rearrange("p r t -> p t r"),
                            ALU.subtract).then_inc(rt, 1)
            dve.wait_ge(rt, 19)
            v.scalar_tensor_tensor(out=c_last_i[:], in0=c_ci[:], scalar=-1.0, in1=c_last[:], op0=ALU.add, op1=ALU.add)
            v.tensor_scalar(c_sel_i[:], c_sel[:], float(R - 1), None, ALU.min).then_inc(rt, 1)
            v.tensor_tensor(c_q2[:], ps_c[0][:, 0:TA * R].rearrange("p (t r) -> p t r", r=R), c_q[:],
                            ALU.add).then_inc(rt, 1)
            dve.wait_ge(rt, 21)
            v.tensor_tensor(c_q[:], c_q2[:], c_sh[:].rearrange("p (a r) -> p a r", a=1).to_broadcast([P, TA, R]),
                            ALU.add).then_inc(rt, 1)
            dve.wait_ge(rt, 22)
            v.tensor_tensor(c_q2[:], c_q[:], c_one[:], ALU.mult).then_inc(rt, 1)
            dve.wait_ge(rt, 23)
            v.tensor_reduce(c_pos[:], c_q2[:], AX.X, ALU.add).then_inc(rt, 1)
            dve.wait_ge(rt, 24)
            v.tensor_copy(c_pos_i[:], c_pos[:]).then_inc(conv_table, 1)

            def rows_a(at):
                j = at(0)
                if j:
                    dve.wait_ge(a_copied, j.n + 1)
                    need(dve, a_mean, j.n - 3)
                    v.bn_stats(a_st[:, j.p], a_row[:, j.p, 0:C]).then_inc(a_stat, 1)
                    done, freed = value(dve, j.n + 1), value(dve, j.n - 3)
                    own_wait(dve)
                    dve.wait_ge(a_stat, done)
                    need(dve, a_meta, freed)
                    v.bn_aggr(a_mv[:, j.p], a_st[:, j.p]).then_inc(a_mean, 1)
                j = at(1)
                if j:
                    if not (isinstance(j.n, int) and j.n < 4):
                        dve.wait_ge(a_sent[j.p], j.h * 16)
                    v.tensor_copy(a_pi[:, j.p], c_pos[:, bass.ds(j.n, 1)])
                    v.tensor_copy(a_row[:, j.p, C:C + 1], tok_id[:, bass.ds(j.n, 1)])
                    dve.wait_ge(a_std, j.n + 1)
                    v.reciprocal(a_row[:, j.p, C + 2:C + 3], a_sd[:, j.p]).then_inc(a_rstd, 1)
                    dve.wait_ge(a_rstd, j.n + 1)
                    v.tensor_scalar(a_row[:, j.p, C + 3:C + 4], a_mv[:, j.p, 0:1], a_row[:, j.p, C + 2:C + 3], -1.0,
                                    ALU.mult, ALU.mult).then_inc(a_meta, 1)

            pipeline(dve, TA, 4, 0, 1, rows_a)

            def rows_b(at):
                j = at(0)
                if j:
                    dve.wait_ge(b_conv, j.n + 1)
                    dve.wait_ge(b_in[j.p], j.h * 16 + 16)
                    need(dve, b_thd, j.n - 3)
                    if not (isinstance(j.n, int) and j.n < 4):
                        dve.wait_ge(t_out[j.p], j.h * 16)
                    v.tensor_tensor(b_t[:, j.p], ps_c[j.p % 2][:, 0:C], b_row[:, j.p, 0:C],
                                    ALU.add).then_inc(b_tsum, 1)
                    dve.wait_ge(b_tsum, j.n + 1)
                    v.bn_stats(b_st[:, j.p], b_t[:, j.p]).then_inc(b_stat, 1)
                    done = value(dve, j.n + 1)
                    own_wait(dve)
                    dve.wait_ge(b_stat, done)
                    v.bn_aggr(b_mv[:, j.p], b_st[:, j.p]).then_inc(b_mean, 1)
                i = at(1)
                if i:
                    dve.wait_ge(b_ttr, i.n + 1)
                    v.tensor_copy(b_tT[:, i.p], ps_t[i.p % 2][:, 0:C]).then_inc(b_tcp, 1)
                if j:
                    dve.wait_ge(b_std, j.n + 1)
                    v.reciprocal(b_rs[:, j.p], b_sd[:, j.p]).then_inc(b_rstd, 1)
                    dve.wait_ge(b_rstd, j.n + 1)
                    v.tensor_scalar(b_nm[:, j.p], b_mv[:, j.p, 0:1], b_rs[:, j.p], -1.0, ALU.mult,
                                    ALU.mult).then_inc(b_nmr, 1)
                if i:
                    dve.wait_ge(b_gate, i.n + 1)
                    v.tensor_tensor(b_lg[:, i.p], ps_g[:, 0:E], gb[:],
                                    ALU.add).then_inc(b_log, 1)
                    v.tensor_scalar(b_bad[:, i.p], b_row[:, i.p, C + 1:C + 2], -INVALID, INVALID, ALU.mult,
                                    ALU.add).then_inc(b_wrong, 1)
                    done = value(dve, i.n + 1)
                    own_wait(dve)
                    dve.wait_ge(b_log, done)
                    v.max(b_m8[:, i.p], b_lg[:, i.p]).then_inc(b_max, 1)
                    done = value(dve, i.n + 1)
                    own_wait(dve)
                    dve.wait_ge(b_max, done)
                    v.max_index(b_i8[:, i.p], b_m8[:, i.p], b_lg[:, i.p]).then_inc(b_idx, 1)
                    dve.wait_ge(b_idx, i.n + 1)
                    dve.wait_ge(b_wrong, i.n + 1)
                    v.tensor_scalar(b_if[:, i.p], b_i8[:, i.p, 0:2], b_bad[:, i.p], None,
                                    ALU.add).then_inc(b_idf, 1)
                    dve.wait_ge(b_idf, i.n + 1)
                    v.tensor_tensor(b_one[:, i.p],
                                    b_if[:, i.p].rearrange("p (k a) -> p k a", a=1).to_broadcast([P, 2, E]),
                                    iota_e[:].rearrange("p (a e) -> p a e", a=1).to_broadcast([P, 2, E]),
                                    ALU.is_equal).then_inc(b_hot, 1)
                    if not (isinstance(i.n, int) and i.n < 4):
                        dve.wait_ge(b_sent[i.p], i.h * 32)
                    v.tensor_copy(b_th[:, i.p, C:C + 1], b_row[:, i.p, C:C + 1])
                    v.tensor_copy(b_th[:, i.p, C + 1:C + 2], b_if[:, i.p, 0:1])
                    v.tensor_tensor(b_th[:, i.p, C + 2:C + 3], b_m8[:, i.p, 0:1], b_m8[:, i.p, 1:2],
                                    ALU.subtract).then_inc(b_meta, 1)
                    dve.wait_ge(b_hot, i.n + 1)
                    v.tensor_tensor(b_cnt[:, i.p], b_one[:, i.p, 0], b_one[:, i.p, 1], ALU.add).then_inc(b_cn, 1)
                    dve.wait_ge(b_cn, i.n + 1)
                    need(dve, b_ac, i.n)
                    need(dve, b_rank, i.n - 2)
                    v.tensor_tensor(b_acc[:, i.p], b_acc[:, (i.p + 3) % 4], b_cnt[:, i.p], ALU.add).then_inc(b_ac, 1)
                j = at(2)
                if j:
                    dve.wait_ge(b_rank, j.n + 1)
                    v.tensor_tensor(b_pr[:, j.p], ps_r[:, 0:E], expert_base[:],
                                    ALU.add).then_inc(b_prs, 1)
                    dve.wait_ge(b_prs, j.n + 1)
                    v.tensor_tensor(b_pq[:, j.p], b_one[:, j.p],
                                    b_pr[:, j.p].rearrange("p (a e) -> p a e", a=1).to_broadcast([P, 2, E]),
                                    ALU.mult).then_inc(b_pqs, 1)
                    dve.wait_ge(b_pqs, j.n + 1)
                    v.tensor_reduce(b_ps[:, j.p], b_pq[:, j.p], AX.X, ALU.add).then_inc(b_pos, 1)
                    dve.wait_ge(b_pos, j.n + 1)
                    v.tensor_scalar(b_pi[:, j.p], b_ps[:, j.p], b_bad[:, j.p], None, ALU.add).then_inc(b_posi, 1)

            pipeline(dve, SB, 4, 0, 2, rows_b)

            dve.wait_ge(totals, 1)
            v.tensor_copy(e_n[:, 0:E], ps_r[:, 0:E]).then_inc(et, 1)
            dve.wait_ge(et, 1)
            v.tensor_tensor(e_pad[:], e_n[:], pad_base[:], ALU.add).then_inc(pads_known, 1)
            v.tensor_scalar(e_ti[:], e_n[:, 0:E], float(P - 1), None, ALU.add).then_inc(et, 1)
            dve.wait_ge(et, 2)
            v.tensor_scalar(e_t2[:], e_ti[:], 7, None, ALU.arith_shift_right).then_inc(et, 1)
            dve.wait_ge(et, 3)
            v.tensor_scalar(e_tf[:], e_t2[:], 1.0, None, ALU.max).then_inc(et, 1)
            dve.wait_ge(et, 4)
            v.tensor_tensor_scan(e_inc[:], c_ones[:, 0:E], e_tf[:], 0.0, ALU.mult, ALU.add).then_inc(et, 1)
            dve.wait_ge(et, 5)
            v.tensor_copy(e_inc_i[:], e_inc[:]).then_inc(et, 1)
            v.tensor_tensor(e_cmp[:], e_inc[:].rearrange("p (a e) -> p a e", a=1).to_broadcast([P, SE, E]),
                            iota_s[:].rearrange("p (s a) -> p s a", a=1).to_broadcast([P, SE, E]),
                            ALU.is_le).then_inc(et, 1)
            dve.wait_ge(et, 7)
            v.tensor_reduce(e_of[:], e_cmp[:], AX.X, ALU.add).then_inc(et, 1)
            v.tensor_tensor(e_cmt[:], e_cmp[:], e_tf[:].rearrange("p (a e) -> p a e", a=1).to_broadcast([P, SE, E]),
                            ALU.mult).then_inc(et, 1)
            dve.wait_ge(et, 9)
            v.tensor_reduce(e_st[:], e_cmt[:], AX.X, ALU.add).then_inc(et, 1)
            v.tensor_scalar(e_clip[:], e_of[:], float(E - 1), None, ALU.min).then_inc(et, 1)
            v.tensor_scalar(e_real[:], e_of[:], float(E), None, ALU.is_lt).then_inc(et, 1)
            v.tensor_scalar(e_adr[:], e_of[:], float(CAP), None, ALU.mult).then_inc(et, 1)
            dve.wait_ge(et, 13)
            v.tensor_copy(e_clip_i[:], e_clip[:]).then_inc(et, 1)
            v.tensor_tensor(e_j[:], iota_s[:], e_st[:], ALU.subtract).then_inc(et, 1)
            dve.wait_ge(et, 15)
            v.tensor_scalar(e_slot_i[:], e_clip_i[:], RING - 1, None, ALU.bitwise_and).then_inc(et, 1)
            v.tensor_tensor(e_j2[:], e_j[:], e_real[:], ALU.mult).then_inc(et, 1)
            dve.wait_ge(et, 17)
            v.scalar_tensor_tensor(out=e_adr_i[:], in0=e_j2[:], scalar=float(P), in1=e_adr[:], op0=ALU.mult,
                                   op1=ALU.add).then_inc(table_known, 1)

            def expert_dve(at):
                j = at(0)
                if j:
                    dve.wait_ge(f_in[j.p], j.h * 16 + 16)
                    need(dve, f_gd, j.n - 3)
                    v.tensor_scalar(f_k1[:, j.p], f_row[:, j.p, C + 1:C + 2], e_of[:, bass.ds(j.n, 1)], None,
                                       ALU.is_equal).then_inc(f_kd, 1)
                    dve.wait_ge(f_kd, j.n + 1)
                    v.tensor_scalar(f_sg[:, j.p], f_k1[:, j.p], 1.0, -0.5, ALU.mult, ALU.add).then_inc(f_sgd, 1)
                    v.tensor_scalar(f_ds[:, j.p], f_k1[:, j.p], -float(TOK), float(TOK), ALU.mult,
                                       ALU.add).then_inc(f_dsd, 1)
                    dve.wait_ge(f_dsd, j.n + 1)
                    if not (isinstance(j.n, int) and j.n < 4):
                        dve.wait_ge(f_sent[j.p], j.h * 16)
                    v.tensor_scalar(f_di[:, j.p], f_ds[:, j.p], f_row[:, j.p, C:C + 1], None,
                                       ALU.add).then_inc(f_did, 1)
                j = at(-1)
                if j:
                    dve.wait_ge(f_xtr, j.n + 1)
                    need(dve, f_h2d, j.n - 1)
                    v.tensor_copy(f_xT[:, j.p % 2], ps_x[j.p % 2][:, 0:C]).then_inc(f_xcp, 1)
                j = at(1)
                if j:
                    dve.wait_ge(f_thd, j.n + 1)
                    v.tensor_scalar(f_g[:, j.p], f_th[:, j.p], 0.5, 0.5, ALU.mult, ALU.add).then_inc(f_gd, 1)
                    dve.wait_ge(f_ymm, j.n + 1)
                    dve.wait_ge(f_gd, j.n + 1)
                    if not (isinstance(j.n, int) and j.n < 4):
                        dve.wait_ge(f_sent[j.p], j.h * 16)
                    v.tensor_scalar(f_y[:, j.p], ps_c[j.p % 2][:, 0:C], f_g[:, j.p], None,
                                    ALU.mult).then_inc(f_yd, 1)
                j = at(0)
                if j:
                    dve.wait_ge(f_sild, j.n + 1)
                    dve.wait_ge(f_h2d, j.n + 1)
                    need(dve, f_htr, j.n - 1)
                    v.tensor_tensor(f_hid[:, j.p % 2], f_sil[:, j.p % 2], ps_h2[:], ALU.mult).then_inc(f_hidd, 1)

            pipeline(dve, SE, 4, 1, 1, expert_dve)

            dve.wait_ge(t_back, 16 * TA)

            def add_out(at):
                j = at(0)
                if j:
                    dve.wait_ge(o_in[j.p], j.h * 32 + 32)
                    v.tensor_tensor(o_s[:, j.p], o_y1[:, j.p], o_y2[:, j.p], ALU.add).then_inc(o_sd, 1)
                    dve.wait_ge(o_sd, j.n + 1)
                    need(dve, o_tr, j.n - 3)
                    v.tensor_tensor(o_r[:, j.p], o_s[:, j.p],
                                    t_tok[:, bass.ds(j.n, 1)].rearrange("p a n -> p (a n)"),
                                    ALU.add).then_inc(o_rd, 1)

            pipeline(dve, TA, 4, 0, 0, add_out)


_INS = ["x", "L0_conv_indexes", "L0_conv_weight", "L0_conv_bias", "L0_ffn_gate_w", "L0_ffn_gate_b",
        "L0_ffn_w1", "L0_ffn_w2", "L0_ffn_w3"]


def kernel(**inputs):
    import numpy as _np
    import concourse.bacc as _bacc
    from concourse import mybir as _mybir
    from concourse.bass_utils import run_bass_kernel_spmd as _run

    nc = _bacc.Bacc("TRN2", target_bir_lowering=False, num_devices=1)
    arrays, args = {}, []
    for name in _INS:
        a = _np.ascontiguousarray(inputs[name])
        arrays[f"in_{name}_dram"] = a
        args.append(nc.dram_tensor(f"in_{name}_dram", a.shape, _mybir.dt.from_np(a.dtype), kind="ExternalInput").ap())
    shape = tuple(inputs["x"].shape)
    args.append(nc.dram_tensor("out_0_dram", shape, _mybir.dt.float32, kind="ExternalOutput").ap())
    metaformer_layer(nc, *args)
    r = _run(nc, [arrays], core_ids=[0])
    return r.results[0]["out_0_dram"]
```
